# Optimizing a Trainium2 kernel written in Bass

```python
import numpy as np
import jax
import jax.numpy as jnp

def _softmax(x, axis=-1):
    return jax.nn.softmax(x, axis=axis)

def _gelu(x):
    return jax.nn.gelu(x, approximate=True)

def _silu(x):
    return jax.nn.silu(x)

def _sigmoid(x):
    return jax.nn.sigmoid(x)

def _layernorm(x, axis=-1, eps=1e-05):
    m = jnp.mean(x, axis=axis, keepdims=True)
    v = jnp.var(x, axis=axis, keepdims=True)
    return (x - m) / jnp.sqrt(v + eps)

def _scatter_add(tgt, idx, src, axis=0):
    return tgt.at[idx].add(src)

def _segment_sum(src, seg, n):
    return jax.ops.segment_sum(src, seg, n)
kernel_name = 'mk_dlrm_tower_d1_rec_r8_a50d77'

def setup_inputs(seed: int=0):
    np.random.seed(seed)
    _w = jnp.asarray

    def _rec_inputs():
        import jax
        import jax.numpy as jnp
        _tk = jax.random.key(seed)
        dense_ctx = jax.random.normal(jax.random.fold_in(_tk, 190), (2048, 16), jnp.float32)
        ids = jnp.stack([jax.random.randint(jax.random.fold_in(_tk, 200 + f), (2048,), 0, v, jnp.int32) for f, v in enumerate([125000, 12500, 1250, 12500, 1000, 125000, 12500, 1000, 1000, 1250, 1250, 125000, 1250, 12500, 1000, 1250, 1000, 12500, 1250, 12500, 1000, 12500, 12500, 1250, 1000, 1250, 1000, 1250, 1000, 1000, 1000, 1000])], axis=1)
        tbl_0 = 0.05 * jax.random.normal(jax.random.fold_in(_tk, 500 + 0), (125000, 64), jnp.float32)
        tbl_1 = 0.05 * jax.random.normal(jax.random.fold_in(_tk, 500 + 1), (12500, 64), jnp.float32)
        tbl_2 = 0.05 * jax.random.normal(jax.random.fold_in(_tk, 500 + 2), (1250, 64), jnp.float32)
        tbl_3 = 0.05 * jax.random.normal(jax.random.fold_in(_tk, 500 + 3), (12500, 64), jnp.float32)
        tbl_4 = 0.05 * jax.random.normal(jax.random.fold_in(_tk, 500 + 4), (1000, 64), jnp.float32)
        tbl_5 = 0.05 * jax.random.normal(jax.random.fold_in(_tk, 500 + 5), (125000, 64), jnp.float32)
        tbl_6 = 0.05 * jax.random.normal(jax.random.fold_in(_tk, 500 + 6), (12500, 64), jnp.float32)
        tbl_7 = 0.05 * jax.random.normal(jax.random.fold_in(_tk, 500 + 7), (1000, 64), jnp.float32)
        tbl_8 = 0.05 * jax.random.normal(jax.random.fold_in(_tk, 500 + 8), (1000, 64), jnp.float32)
        tbl_9 = 0.05 * jax.random.normal(jax.random.fold_in(_tk, 500 + 9), (1250, 64), jnp.float32)
        tbl_10 = 0.05 * jax.random.normal(jax.random.fold_in(_tk, 500 + 10), (1250, 64), jnp.float32)
        tbl_11 = 0.05 * jax.random.normal(jax.random.fold_in(_tk, 500 + 11), (125000, 64), jnp.float32)
        tbl_12 = 0.05 * jax.random.normal(jax.random.fold_in(_tk, 500 + 12), (1250, 64), jnp.float32)
        tbl_13 = 0.05 * jax.random.normal(jax.random.fold_in(_tk, 500 + 13), (12500, 64), jnp.float32)
        tbl_14 = 0.05 * jax.random.normal(jax.random.fold_in(_tk, 500 + 14), (1000, 64), jnp.float32)
        tbl_15 = 0.05 * jax.random.normal(jax.random.fold_in(_tk, 500 + 15), (1250, 64), jnp.float32)
        tbl_16 = 0.05 * jax.random.normal(jax.random.fold_in(_tk, 500 + 16), (1000, 64), jnp.float32)
        tbl_17 = 0.05 * jax.random.normal(jax.random.fold_in(_tk, 500 + 17), (12500, 64), jnp.float32)
        tbl_18 = 0.05 * jax.random.normal(jax.random.fold_in(_tk, 500 + 18), (1250, 64), jnp.float32)
        tbl_19 = 0.05 * jax.random.normal(jax.random.fold_in(_tk, 500 + 19), (12500, 64), jnp.float32)
        tbl_20 = 0.05 * jax.random.normal(jax.random.fold_in(_tk, 500 + 20), (1000, 64), jnp.float32)
        tbl_21 = 0.05 * jax.random.normal(jax.random.fold_in(_tk, 500 + 21), (12500, 64), jnp.float32)
        tbl_22 = 0.05 * jax.random.normal(jax.random.fold_in(_tk, 500 + 22), (12500, 64), jnp.float32)
        tbl_23 = 0.05 * jax.random.normal(jax.random.fold_in(_tk, 500 + 23), (1250, 64), jnp.float32)
        tbl_24 = 0.05 * jax.random.normal(jax.random.fold_in(_tk, 500 + 24), (1000, 64), jnp.float32)
        tbl_25 = 0.05 * jax.random.normal(jax.random.fold_in(_tk, 500 + 25), (1250, 64), jnp.float32)
        tbl_26 = 0.05 * jax.random.normal(jax.random.fold_in(_tk, 500 + 26), (1000, 64), jnp.float32)
        tbl_27 = 0.05 * jax.random.normal(jax.random.fold_in(_tk, 500 + 27), (1250, 64), jnp.float32)
        tbl_28 = 0.05 * jax.random.normal(jax.random.fold_in(_tk, 500 + 28), (1000, 64), jnp.float32)
        tbl_29 = 0.05 * jax.random.normal(jax.random.fold_in(_tk, 500 + 29), (1000, 64), jnp.float32)
        tbl_30 = 0.05 * jax.random.normal(jax.random.fold_in(_tk, 500 + 30), (1000, 64), jnp.float32)
        tbl_31 = 0.05 * jax.random.normal(jax.random.fold_in(_tk, 500 + 31), (1000, 64), jnp.float32)
        _rk = jax.random.fold_in(_tk, 7)
        W_top1 = 0.0441942 * jax.random.normal(jax.random.fold_in(_tk, 801), (512, 512), jnp.float32)
        W_top2 = 0.0441942 * jax.random.normal(jax.random.fold_in(_tk, 802), (512, 256), jnp.float32)
        W_top3 = 0.0625 * jax.random.normal(jax.random.fold_in(_tk, 803), (256, 1), jnp.float32)
        b_top1 = jnp.zeros((512,), jnp.float32)
        b_top2 = jnp.zeros((256,), jnp.float32)
        return (dense_ctx, ids, tbl_0, tbl_1, tbl_2, tbl_3, tbl_4, tbl_5, tbl_6, tbl_7, tbl_8, tbl_9, tbl_10, tbl_11, tbl_12, tbl_13, tbl_14, tbl_15, tbl_16, tbl_17, tbl_18, tbl_19, tbl_20, tbl_21, tbl_22, tbl_23, tbl_24, tbl_25, tbl_26, tbl_27, tbl_28, tbl_29, tbl_30, tbl_31, W_top1, b_top1, W_top2, b_top2, W_top3)
    dense_ctx, ids, tbl_0, tbl_1, tbl_2, tbl_3, tbl_4, tbl_5, tbl_6, tbl_7, tbl_8, tbl_9, tbl_10, tbl_11, tbl_12, tbl_13, tbl_14, tbl_15, tbl_16, tbl_17, tbl_18, tbl_19, tbl_20, tbl_21, tbl_22, tbl_23, tbl_24, tbl_25, tbl_26, tbl_27, tbl_28, tbl_29, tbl_30, tbl_31, W_top1, b_top1, W_top2, b_top2, W_top3 = _rec_inputs()

    def _L0_rec_setup():
        import jax, jax.numpy as jnp
        import numpy as np
        key = jax.random.key(seed)
        k1, k2 = jax.random.split(key)
        B, F, D = (512, 32, 64)
        P = F * (F - 1) // 2
        x = jax.random.normal(k1, (B, F, D), dtype=jnp.float32)
        W = jax.random.normal(k2, (P, D, D), dtype=jnp.float32) * (1.0 / np.sqrt(D))
        return {'x': x, 'W': W}
    _L0_rec_all = _L0_rec_setup()
    _L0_rec_in = {k: v for k, v in _L0_rec_all.items() if k in ('W',)}
    del _L0_rec_all
    return {'dense_ctx': dense_ctx, 'ids': ids, 'tbl_0': tbl_0, 'tbl_1': tbl_1, 'tbl_2': tbl_2, 'tbl_3': tbl_3, 'tbl_4': tbl_4, 'tbl_5': tbl_5, 'tbl_6': tbl_6, 'tbl_7': tbl_7, 'tbl_8': tbl_8, 'tbl_9': tbl_9, 'tbl_10': tbl_10, 'tbl_11': tbl_11, 'tbl_12': tbl_12, 'tbl_13': tbl_13, 'tbl_14': tbl_14, 'tbl_15': tbl_15, 'tbl_16': tbl_16, 'tbl_17': tbl_17, 'tbl_18': tbl_18, 'tbl_19': tbl_19, 'tbl_20': tbl_20, 'tbl_21': tbl_21, 'tbl_22': tbl_22, 'tbl_23': tbl_23, 'tbl_24': tbl_24, 'tbl_25': tbl_25, 'tbl_26': tbl_26, 'tbl_27': tbl_27, 'tbl_28': tbl_28, 'tbl_29': tbl_29, 'tbl_30': tbl_30, 'tbl_31': tbl_31, 'W_top1': W_top1, 'b_top1': b_top1, 'W_top2': W_top2, 'b_top2': b_top2, 'W_top3': W_top3, 'L0_rec_W': _L0_rec_in['W']}

def reference(dense_ctx, ids, tbl_0, tbl_1, tbl_2, tbl_3, tbl_4, tbl_5, tbl_6, tbl_7, tbl_8, tbl_9, tbl_10, tbl_11, tbl_12, tbl_13, tbl_14, tbl_15, tbl_16, tbl_17, tbl_18, tbl_19, tbl_20, tbl_21, tbl_22, tbl_23, tbl_24, tbl_25, tbl_26, tbl_27, tbl_28, tbl_29, tbl_30, tbl_31, W_top1, b_top1, W_top2, b_top2, W_top3, L0_rec_W):
    import jax
    import jax.numpy as jnp

    def _L0_rec_ref(x, W):
        import jax, jax.numpy as jnp
        import numpy as np
        F = x.shape[1]
        idx_i, idx_j = np.triu_indices(F, k=1)
        xi = x[:, idx_i, :]
        xj = x[:, idx_j, :]
        left = jnp.einsum('bpd,pde->bpe', xi, W)
        out = jnp.sum(left * xj, axis=-1)
        return out
    e = jnp.stack([tbl_0[ids[:, 0]], tbl_1[ids[:, 1]], tbl_2[ids[:, 2]], tbl_3[ids[:, 3]], tbl_4[ids[:, 4]], tbl_5[ids[:, 5]], tbl_6[ids[:, 6]], tbl_7[ids[:, 7]], tbl_8[ids[:, 8]], tbl_9[ids[:, 9]], tbl_10[ids[:, 10]], tbl_11[ids[:, 11]], tbl_12[ids[:, 12]], tbl_13[ids[:, 13]], tbl_14[ids[:, 14]], tbl_15[ids[:, 15]], tbl_16[ids[:, 16]], tbl_17[ids[:, 17]], tbl_18[ids[:, 18]], tbl_19[ids[:, 19]], tbl_20[ids[:, 20]], tbl_21[ids[:, 21]], tbl_22[ids[:, 22]], tbl_23[ids[:, 23]], tbl_24[ids[:, 24]], tbl_25[ids[:, 25]], tbl_26[ids[:, 26]], tbl_27[ids[:, 27]], tbl_28[ids[:, 28]], tbl_29[ids[:, 29]], tbl_30[ids[:, 30]], tbl_31[ids[:, 31]]], axis=1)
    z = _L0_rec_ref(e, L0_rec_W)
    z = z.reshape(z.shape[0], -1)
    h = jnp.concatenate([z, dense_ctx], axis=1)
    h = jnp.maximum(h @ W_top1 + b_top1, 0.0)
    h = jnp.maximum(h @ W_top2 + b_top2, 0.0)
    y = h @ W_top3
    return y

_drawn_inputs = setup_inputs


def setup_inputs(seed=0):
    import zlib

    import numpy as np

    out = dict(_drawn_inputs(seed))
    spreads = {'b_top1': (0.0, 0.1), 'b_top2': (0.0, 0.1)}
    factors = {}
    for name, (base, spread) in spreads.items():
        noise = np.random.default_rng([zlib.crc32(name.encode()), seed]).standard_normal(out[name].shape)
        drawn = base * np.exp(spread * noise) if base else spread * noise
        out[name] = jnp.asarray(drawn.astype(out[name].dtype))
    for name, factor in factors.items():
        out[name] = (out[name] * factor).astype(out[name].dtype)
    return out
```

```python
from contextlib import ExitStack

import numpy as np

import concourse.bass as bass
from concourse import mybir

F32 = mybir.dt.float32
F32R = mybir.dt.float32r
U32 = mybir.dt.uint32
ALU = mybir.AluOpType
ACT = mybir.ActivationFunctionType

P = 128
BATCH = 2048
F = 32
D = 64
NB = 256
BLOCKS = BATCH // NB
BANK = 512
SUB = NB // P
PAIRS = F // 2
DENSE = 16
H1, H2 = 512, 256

TILES = [(i, k) for i in range(F - 2, -1, -1) for k in range((i + 1) // 2, PAIRS)]
UNIT = 4
UNITS = len(TILES) // UNIT
ROUNDS = 16
CHUNKS = UNITS // ROUNDS
LSLOTS, PSLOTS = 2, 4
SSLOTS = 4
RAWS = 4
EARLY = 6
WTILES = 8
WCHUNKS = len(TILES) // WTILES
WSTAGES = 3
MLPS = H1 // P + H2 // P + 1

FIRST = {i: min(q for q, t in enumerate(TILES) if t[0] == i) // UNIT for i in range(F - 1)}
LAST = {i: max(q for q, t in enumerate(TILES) if t[0] == i) // UNIT for i in range(F - 1)}

SPLIT_AT = {}
for i in range(F - 2, -1, -1):
    had = LAST[i + SSLOTS] if i + SSLOTS <= F - 2 else LAST[i % SSLOTS] - UNITS
    SPLIT_AT[i] = max(FIRST[i] - 5, had, SPLIT_AT.get(i + 1, -UNITS))
NEED = [n * n // UNIT for n in range(PAIRS)]
START = [SPLIT_AT[min(2 * (PAIRS - 1 - n) + 1, F - 2)] for n in range(PAIRS)]
LOW_AT = [p - 1 for p in START]
HIGH_AT = [p - 2 if n < EARLY else max(p - 2, 0) for n, p in enumerate(START)]
TURN_AT = [-12, -9, -7, -5, -4, -3] + [max(p - 5, 0) for p in START[EARLY:]]
TURN_AT0 = [min(max(0, u - 3), UNITS + TURN_AT[0] - 2) for u in NEED]
HIGH_AT0 = [max(0, u - 2) for u in NEED]
SPLIT_AT0 = {i: HIGH_AT0[PAIRS - 1 - i // 2] for i in range(F - 1)}

L1_AT, L2_AT, L3_AT = 8, 13, 16


def at(places, places0, r, first, last):
    own = places0 if first else places
    order = sorted(own, reverse=True) if isinstance(own, dict) else range(len(own))
    due = [(n, 0) for n in order if own[n] == r and own[n] >= 0]
    if not last:
        due += [(n, 1) for n in order if places[n] < 0 and places[n] + UNITS == r]
    return due


def dlrm_kernel(nc, ids, tables, w_pairs, dense_t, w_top1, w_dense, b_top1, w_top2, b_top2, w_top3,
                ident_in, sel_in, out):
    ctx = ExitStack()
    with ctx:
        def sb(name, cols, dt=F32):
            return ctx.enter_context(nc.sbuf_tensor(name, [P, cols], dt))

        def ps(name, cols):
            return ctx.enter_context(nc.psum_tensor(name, [P, cols], F32))

        def sem(name):
            return ctx.enter_context(nc.semaphore(name))

        w_split = sb("w_split", len(TILES) * P, F32R)
        late = sb("late", (EARLY + H1 // P + H2 // P) * NB)
        x_main = sb("x_main", PAIRS * NB)
        raw = sb("raw", RAWS * SUB * P)
        x_high = sb("x_high", NB, F32R)
        x_low = sb("x_low", 2 * NB)
        s_high = sb("s_high", SSLOTS * NB, F32R)
        s_low = sb("s_low", SSLOTS * NB, F32R)
        prods = sb("prods", PSLOTS * UNIT * NB)
        z = sb("z", CHUNKS * NB)
        dense = sb("dense", NB)
        w1 = sb("w1", CHUNKS * H1)
        w1d = sb("w1d", H1)
        w2 = sb("w2", (H1 // P) * H2)
        w3 = sb("w3", H2 // P)
        b1 = sb("b1", H1 // P)
        b2 = sb("b2", H2 // P)
        ident = sb("ident", P)
        sel = sb("sel", 62)
        idx = sb("idx", SUB * F, U32)
        h1 = late[:, EARLY * NB:(EARLY + H1 // P) * NB]
        h2 = late[:, (EARLY + H1 // P) * NB:]
        y = h2[0:1, 0:NB]
        wcols = WTILES * P

        left = ps("left", LSLOTS * UNIT * NB)
        z_sum = ps("z_sum", 2 * BANK)
        turned = ps("turned", BANK)
        mlp = ps("mlp", BANK)

        consts_in = sem("consts_in")
        top_in = sem("top_in")
        zeroed = sem("zeroed")
        ids_in = sem("ids_in")
        slot_free = sem("slot_free")
        dense_in = sem("dense_in")
        gathered = [sem(f"gathered{s}") for s in range(RAWS)]
        w_in = [sem(f"w_in{s}") for s in range(WSTAGES)]
        w_rounded = sem("w_rounded")
        w_ready = sem("w_ready")
        x_turned = sem("x_turned")
        x_ready = sem("x_ready")
        high_ready = sem("high_ready")
        low_ready = sem("low_ready")
        s_ready = sem("s_ready")
        left_ready = sem("left_ready")
        prods_ready = sem("prods_ready")
        prods_summed = sem("prods_summed")
        z_ready = sem("z_ready")
        mlp_out = sem("mlp_out")
        mlp_taken = sem("mlp_taken")
        y_out = sem("y_out")

        def x_at(k, parity):
            if parity and k >= PAIRS - EARLY:
                return late, (k - (PAIRS - EARLY)) * NB
            return x_main, k * NB

        def x_pair(k, parity):
            tensor, c = x_at(k, parity)
            return tensor[:, c:c + NB]

        def before(sem_count, first, count):
            return not first or sem_count + count > 0

        block = ctx.enter_context(nc.Block())

        @block.sync
        def _(sp):
            sp.dma_start(ident[:, :], ident_in).then_inc(consts_in, 16)
            sp.dma_start(sel[:, :], sel_in).then_inc(consts_in, 16)
            for c in range(WCHUNKS):
                stage = late[:, (c % WSTAGES) * wcols:(c % WSTAGES + 1) * wcols]
                if c >= WSTAGES:
                    sp.wait_ge(w_ready, c - WSTAGES + 1)
                for half in (0, D):
                    sp.dma_start(stage[half:half + D, :], w_pairs[:, c * wcols:(c + 1) * wcols])\
                        .then_inc(w_in[c % WSTAGES], 16)
            sp.dma_start(w1[:, :].rearrange("p (c n) -> p c n", c=CHUNKS),
                         w_top1.rearrange("(c p) n -> p c n", p=P)).then_inc(top_in, 16)
            sp.dma_start(w2[:, :].rearrange("p (c n) -> p c n", c=H1 // P),
                         w_top2.rearrange("(c p) n -> p c n", p=P)).then_inc(top_in, 16)
            sp.dma_start(w3[:, :], w_top3).then_inc(top_in, 16)
            sp.dma_start(b1[:, :], b_top1).then_inc(top_in, 16)
            sp.dma_start(b2[:, :], b_top2).then_inc(top_in, 16)
            sp.wait_ge(zeroed, 2)
            sp.dma_start(w1d[0:DENSE, :], w_dense).then_inc(top_in, 16)
            sp.dma_start(dense[0:DENSE, :], dense_t[:, 0:NB]).then_inc(dense_in, 16)
            with sp.Fori(1, BLOCKS) as t:
                sp.wait_ge(mlp_out, t * MLPS - MLPS + H1 // P)
                sp.dma_start(dense[0:DENSE, :], dense_t[:, bass.ds(t * NB, NB)]).then_inc(dense_in, 16)
                sp.wait_ge(mlp_taken, t * MLPS)
                sp.dma_start(out[:, bass.ds(t * NB - NB, NB)], y).then_inc(y_out, 16)
            sp.wait_ge(mlp_taken, BLOCKS * MLPS)
            sp.dma_start(out[:, (BLOCKS - 1) * NB:], y).then_inc(y_out, 16)
            sp.wait_ge(y_out, 16 * BLOCKS)

        @block.gpsimd
        def _(pool):
            def gather_block(t, first):
                if not first:
                    for s in range(RAWS):
                        pool.wait_ge(gathered[s], t * (PAIRS // RAWS * 2 * SUB * 16))
                pool.dma_start(idx[:, :], ids[0] if first else ids[bass.ds(t, 1), :, :].rearrange(
                    "a p c -> (a p) c")).then_inc(ids_in, 16)
                pool.wait_ge(ids_in, 16 if first else t * 16 + 16)
                for n in range(PAIRS):
                    if not first or n >= RAWS:
                        pool.wait_ge(x_turned, n - RAWS + 1 if first else t * PAIRS + (n - RAWS + 1))
                    pool.sem_inc(slot_free, 1)
                    for h in range(2):
                        f = 2 * (PAIRS - 1 - n) + h
                        for s in range(SUB):
                            c = ((n % RAWS) * SUB + s) * P + h * D
                            pool.indirect_dma_start(
                                raw[:, c:c + D], None, tables[f],
                                bass.IndirectOffsetOnAxis(ap=idx[:, f * SUB + s:f * SUB + s + 1], axis=0),
                            ).then_inc(gathered[n % RAWS], 16)

            gather_block(0, True)
            with pool.Fori(1, BLOCKS) as t:
                gather_block(t, False)

        @block.tensor
        def _(pe):
            def turn(t, n, ahead):
                g = (t + ahead) * PAIRS + n
                pe.wait_ge(gathered[n % RAWS], (t + ahead) * (PAIRS // RAWS * 2 * SUB * 16)
                           + (n // RAWS + 1) * 2 * SUB * 16)
                if not isinstance(g, int) or g >= 1:
                    pe.wait_ge(x_ready, g)
                for s in range(SUB):
                    c = ((n % RAWS) * SUB + s) * P
                    last = nc.tensor.transpose(turned[:, s * P:(s + 1) * P],
                                               raw[:, c:c + P], ident[:, :])
                last.then_inc(x_turned, 1)

            def multiply(t, r, first):
                if first and r % (WTILES // UNIT) == 0:
                    pe.wait_ge(w_ready, r // (WTILES // UNIT) + 1)
                if not first or r >= LSLOTS:
                    pe.wait_ge(prods_ready, t * UNITS + (r - LSLOTS + 1))
                for a in range(UNIT):
                    q = r * UNIT + a
                    i = TILES[q][0]
                    if a == 0 or i != TILES[q - 1][0]:
                        pe.wait_ge(s_ready, t * (F - 1) + (F - 1 - i))
                    o = left[:, ((r % LSLOTS) * UNIT + a) * NB:((r % LSLOTS) * UNIT + a + 1) * NB]
                    w = w_split[:, q * P:(q + 1) * P]
                    c = (i % SSLOTS) * NB
                    nc.tensor.matmul(o, w, s_high[:, c:c + NB], start=True, stop=False)
                    last = nc.tensor.matmul(o, w, s_low[:, c:c + NB], start=False, stop=True)
                last.then_inc(left_ready, 1)

            def reduce(t, r, first):
                c, s = divmod(r, ROUNDS)
                if s == 0 and (not first or c >= 2):
                    pe.wait_ge(z_ready, t * CHUNKS + (c - 1))
                pe.wait_ge(prods_ready, t * UNITS + (r + 1))
                for g in range(UNIT):
                    last = nc.tensor.matmul(z_sum[32 * g:32 * g + 32, (c % 2) * BANK:(c % 2) * BANK + NB],
                                            sel[:, 30 - 2 * s:62 - 2 * s],
                                            prods[:, ((r % PSLOTS) * UNIT + g) * NB:((r % PSLOTS) * UNIT + g + 1) * NB],
                                            start=(s == 0), stop=(s == ROUNDS - 1))
                last.then_inc(prods_summed, 1)

            def layer1(t, j, once):
                if j == 0:
                    if once:
                        pe.wait_ge(top_in, 16 * 6)
                    pe.wait_ge(z_ready, t * CHUNKS + CHUNKS)
                    pe.wait_ge(dense_in, t * 16 + 16)
                if not once or j:
                    pe.wait_ge(mlp_taken, t * MLPS + j)
                for c in range(CHUNKS):
                    nc.tensor.matmul(mlp[:, 0:NB], w1[:, c * H1 + j * P:c * H1 + (j + 1) * P],
                                     z[:, c * NB:(c + 1) * NB], start=(c == 0), stop=False)
                nc.tensor.matmul(mlp[:, 0:NB], w1d[:, j * P:(j + 1) * P], dense[:, :], start=False, stop=True)\
                    .then_inc(mlp_out, 1)

            def layer2(t, j):
                pe.wait_ge(mlp_taken, t * MLPS + (H1 // P + j))
                for c in range(H1 // P):
                    last = nc.tensor.matmul(mlp[:, 0:NB], w2[:, c * H2 + j * P:c * H2 + (j + 1) * P],
                                            h1[:, c * NB:(c + 1) * NB], start=(c == 0), stop=(c == H1 // P - 1))
                last.then_inc(mlp_out, 1)

            def layer3(t):
                pe.wait_ge(mlp_taken, t * MLPS + H1 // P + H2 // P)
                for c in range(H2 // P):
                    last = nc.tensor.matmul(mlp[0:1, 0:NB], w3[:, c:c + 1], h2[:, c * NB:(c + 1) * NB],
                                            start=(c == 0), stop=(c == H2 // P - 1))
                last.then_inc(mlp_out, 1)

            def top(t, r, once):
                if L1_AT <= r < L1_AT + H1 // P:
                    layer1(t, r - L1_AT, once)
                if L2_AT <= r < L2_AT + H2 // P:
                    layer2(t, r - L2_AT)
                if r == L3_AT:
                    layer3(t)

            def run_block(t, first=False, last=False, once=False):
                for r in range(UNITS):
                    for n, ahead in at(TURN_AT, TURN_AT0, r, first, last):
                        turn(t, n, ahead)
                    multiply(t, r, first)
                    if r % 2:
                        for d in (3, 2):
                            if r >= d:
                                reduce(t, r - d, first)
                            elif not first:
                                reduce(t - 1, r - d + UNITS, once)
                    if not first:
                        top(t - 1, r, once)

            pe.wait_ge(consts_in, 32)
            run_block(0, first=True)
            run_block(1, once=True)
            with pe.Fori(2, BLOCKS - 1) as t:
                run_block(t)
            run_block(BLOCKS - 1, last=True)
            for r in (UNITS - 2, UNITS - 1):
                reduce(BLOCKS - 1, r, False)
            for r in range(UNITS):
                top(BLOCKS - 1, r, False)

        @block.scalar
        def _(act):
            def round_w(c):
                act.wait_ge(w_in[c % WSTAGES], (c // WSTAGES + 1) * 32)
                nc.scalar.copy(w_split[:, c * wcols:(c + 1) * wcols],
                               late[:, (c % WSTAGES) * wcols:(c % WSTAGES + 1) * wcols]).then_inc(w_rounded, 1)

            def take_x(t, n, ahead, parity, first):
                k = PAIRS - 1 - n
                g = (t + ahead) * PAIRS + n
                act.wait_ge(x_turned, g + 1)
                if ahead and first:
                    act.wait_ge(w_ready, WCHUNKS)
                elif not first:
                    act.wait_ge(prods_ready, (t - 1 + ahead) * UNITS if ahead else t * UNITS)
                nc.scalar.copy(x_pair(k, (parity + ahead) % 2), turned[:, 0:NB])\
                    .then_inc(x_ready, 1)

            def high(t, n, ahead, parity):
                g = (t + ahead) * PAIRS + n
                act.wait_ge(x_ready, g + 1)
                if not isinstance(g, int) or g >= 1:
                    act.wait_ge(low_ready, g)
                nc.scalar.copy(x_high[:, :], x_pair(PAIRS - 1 - n, (parity + ahead) % 2)).then_inc(high_ready, 1)

            def split(t, i, ahead, parity, first):
                n = PAIRS - 1 - i // 2
                x = x_pair(i // 2, (parity + ahead) % 2)
                c = (i % SSLOTS) * NB
                rows = slice(D, P) if i % 2 else slice(0, D)
                if i + SSLOTS <= F - 2:
                    act.wait_ge(left_ready, (t + ahead) * UNITS + (LAST[i + SSLOTS] + 1))
                elif not (first and not ahead):
                    act.wait_ge(left_ready, (t + ahead) * UNITS + (LAST[i % SSLOTS] + 1 - UNITS))
                nc.scalar.copy(s_high[0:D, c:c + NB], x[rows, :])
                nc.scalar.copy(s_high[D:P, c:c + NB], x[rows, :])
                act.wait_ge(low_ready, (t + ahead) * PAIRS + (n + 1))
                low = x_low[rows, (n % 2) * NB:(n % 2 + 1) * NB]
                nc.scalar.copy(s_low[0:D, c:c + NB], low)
                nc.scalar.copy(s_low[D:P, c:c + NB], low).then_inc(s_ready, 1)

            def take_z(t, c, once):
                act.wait_ge(prods_summed, t * UNITS + (c + 1) * ROUNDS)
                if not once:
                    act.wait_ge(mlp_out, (t - 1) * MLPS + H1 // P)
                nc.scalar.copy(z[:, c * NB:(c + 1) * NB], z_sum[:, (c % 2) * BANK:(c % 2) * BANK + NB])\
                    .then_inc(z_ready, 1)

            def relu(t, m, once):
                act.wait_ge(mlp_out, t * MLPS + (m + 1))
                if once and m == 0:
                    act.wait_ge(w_ready, WCHUNKS)
                if m < H1 // P:
                    nc.scalar.activation(h1[:, m * NB:(m + 1) * NB], mlp[:, 0:NB], ACT.Relu, bias=b1[:, m:m + 1])\
                        .then_inc(mlp_taken, 1)
                else:
                    j = m - H1 // P
                    if not once:
                        act.wait_ge(y_out, t * 16)
                    nc.scalar.activation(h2[:, j * NB:(j + 1) * NB], mlp[:, 0:NB], ACT.Relu, bias=b2[:, j:j + 1]).then_inc(mlp_taken, 1)

            def take_y(t, once):
                act.wait_ge(mlp_out, t * MLPS + MLPS)
                nc.scalar.copy(y, mlp[0:1, 0:NB]).then_inc(mlp_taken, 1)

            def top(t, r, once):
                if L1_AT + 1 <= r < L1_AT + 1 + H1 // P:
                    relu(t, r - L1_AT - 1, once)
                if L2_AT + 1 <= r < L2_AT + 1 + H2 // P:
                    relu(t, r - L2_AT - 1 + H1 // P, once)
                if r == L3_AT + 1:
                    take_y(t, once)

            def run_block(t, parity, first=False, last=False, once=False):
                for r in range(UNITS):
                    if first:
                        for c in range(WCHUNKS):
                            if W_AT[c] == r:
                                round_w(c)
                    for n, ahead in at(TURN_AT, TURN_AT0, r, first, last):
                        take_x(t, n, ahead, parity, first)
                    highs = at(HIGH_AT, HIGH_AT0, r, first, last)
                    splits = at(SPLIT_AT, SPLIT_AT0, r, first, last)
                    for i, ahead in splits:
                        if (PAIRS - 1 - i // 2, ahead) not in highs:
                            split(t, i, ahead, parity, first)
                    for n, ahead in highs:
                        high(t, n, ahead, parity)
                        for i, far in splits:
                            if (PAIRS - 1 - i // 2, far) == (n, ahead):
                                split(t, i, far, parity, first)
                    if r == 2 and not first:
                        take_z(t - 1, CHUNKS - 1, once)
                    if r > 2 and r % ROUNDS == 2:
                        take_z(t, r // ROUNDS - 1, first)
                    if not first:
                        top(t - 1, r, once)

            run_block(0, 0, first=True)
            run_block(1, 1, once=True)
            with act.Fori(2, BLOCKS - 2, 2) as t:
                run_block(t, 0)
                run_block(t + 1, 1)
            run_block(BLOCKS - 2, 0)
            run_block(BLOCKS - 1, 1, last=True)
            take_z(BLOCKS - 1, CHUNKS - 1, False)
            for r in range(UNITS):
                top(BLOCKS - 1, r, False)

        @block.vector
        def _(dve):
            def split_w(c):
                dve.wait_ge(w_rounded, c + 1)
                cols = slice(c * wcols, (c + 1) * wcols)
                nc.vector.tensor_tensor(w_split[D:P, cols],
                                        late[D:P, (c % WSTAGES) * wcols:(c % WSTAGES + 1) * wcols],
                                        w_split[D:P, cols].bitcast(F32), ALU.subtract).then_inc(w_ready, 1)

            def low(t, n, ahead, parity, first):
                g = (t + ahead) * PAIRS + n
                dve.wait_ge(high_ready, g + 1)
                if n >= 2:
                    dve.wait_ge(s_ready, (t + ahead) * (F - 1) + 2 * (n - 2) + 1)
                elif not (first and not ahead):
                    dve.wait_ge(s_ready, (t + ahead) * (F - 1) + 2 * (n - 2))
                nc.vector.tensor_tensor(x_low[:, (n % 2) * NB:(n % 2 + 1) * NB],
                                        x_pair(PAIRS - 1 - n, (parity + ahead) % 2),
                                        x_high[:, :].bitcast(F32), ALU.subtract).then_inc(low_ready, 1)

            def products(t, r, parity, first):
                dve.wait_ge(left_ready, t * UNITS + (r + 1))
                if not first or r >= PSLOTS:
                    dve.wait_ge(prods_summed, t * UNITS + (r - PSLOTS + 1))
                a = 0
                while a < UNIT:
                    tensor, c = x_at(TILES[r * UNIT + a][1], parity)
                    b = a + 1
                    while b < UNIT:
                        tb, cb = x_at(TILES[r * UNIT + b][1], parity)
                        if tb is not tensor or cb != c + (b - a) * NB:
                            break
                        b += 1
                    o, l = (r % PSLOTS) * UNIT, (r % LSLOTS) * UNIT
                    last = nc.vector.tensor_tensor(prods[:, (o + a) * NB:(o + b) * NB],
                                                   left[:, (l + a) * NB:(l + b) * NB],
                                                   tensor[:, c:c + (b - a) * NB], ALU.mult)
                    a = b
                last.then_inc(prods_ready, 1)

            def run_block(t, parity, first=False, last=False):
                for r in range(UNITS):
                    if first:
                        for c in range(WCHUNKS):
                            if W_AT[c] == r:
                                split_w(c)
                    for n, ahead in at(LOW_AT, HIGH_AT0, r, first, last):
                        low(t, n, ahead, parity, first)
                    products(t, r, parity, first)

            nc.vector.memset(w1d[:, :], 0.0).then_inc(zeroed, 1)
            nc.vector.memset(dense[:, :], 0.0).then_inc(zeroed, 1)
            run_block(0, 0, first=True)
            with dve.Fori(1, BLOCKS - 1, 2) as t:
                run_block(t, 1)
                run_block(t + 1, 0)
            run_block(BLOCKS - 1, 1, last=True)


W_AT = [max(0, int(1.4 * c) - 2) for c in range(WCHUNKS)]


def pair_number(i, j):
    return i * (F - 1) - i * (i - 1) // 2 + (j - i - 1)


def kernel(**inputs):
    import concourse.bacc as bacc
    from concourse.bass_utils import run_bass_kernel_spmd

    w = inputs["L0_rec_W"]
    w_pairs = np.zeros((D, len(TILES), 2, D), w.dtype)
    w_top1 = np.zeros((CHUNKS * P, H1), w.dtype)
    for q, (i, k) in enumerate(TILES):
        for h in range(2):
            if 2 * k + h > i:
                p = pair_number(i, 2 * k + h)
                w_pairs[:, q, h, :] = w[p]
                c, s, g = q // (UNIT * ROUNDS), q // UNIT % ROUNDS, q % UNIT
                w_top1[c * P + 32 * g + 2 * s + h] = inputs["W_top1"][p]
    sel = np.zeros((P, 62), w.dtype)
    sel[:D, 30] = 1
    sel[D:, 31] = 1
    ids = np.ascontiguousarray(inputs["ids"].reshape(BLOCKS, SUB, P, F).transpose(0, 2, 3, 1))
    arrays = {
        "ids": ids.reshape(BLOCKS, P, F * SUB),
        "w_pairs": w_pairs.reshape(D, len(TILES) * P),
        "dense_t": np.ascontiguousarray(inputs["dense_ctx"].T),
        "w_top1": w_top1,
        "w_dense": np.ascontiguousarray(inputs["W_top1"][F * (F - 1) // 2:]),
        "b_top1": np.ascontiguousarray(inputs["b_top1"].reshape(H1 // P, P).T),
        "w_top2": np.ascontiguousarray(inputs["W_top2"]),
        "b_top2": np.ascontiguousarray(inputs["b_top2"].reshape(H2 // P, P).T),
        "w_top3": np.ascontiguousarray(inputs["W_top3"].reshape(H2 // P, P).T),
        "ident": np.eye(P, dtype=w.dtype),
        "sel": sel,
    }
    for f in range(F):
        arrays[f"tbl_{f}"] = np.ascontiguousarray(inputs[f"tbl_{f}"])
    nc = bacc.Bacc("TRN2", target_bir_lowering=False, num_devices=1)
    ap = {}
    for name, a in arrays.items():
        dt = U32 if name == "ids" else mybir.dt.from_np(a.dtype)
        ap[name] = nc.dram_tensor(f"in_{name}", a.shape, dt, kind="ExternalInput").ap()
    out = nc.dram_tensor("out_y", (1, BATCH), F32, kind="ExternalOutput").ap()
    dlrm_kernel(nc, ap["ids"], [ap[f"tbl_{f}"] for f in range(F)], ap["w_pairs"], ap["dense_t"], ap["w_top1"],
                ap["w_dense"], ap["b_top1"], ap["w_top2"], ap["b_top2"], ap["w_top3"], ap["ident"], ap["sel"], out)
    arrays["ids"] = arrays["ids"].view(np.uint32)
    result = run_bass_kernel_spmd(nc, [{f"in_{k}": v for k, v in arrays.items()}], core_ids=[0])
    return result.results[0]["out_y"].reshape(BATCH, 1)
```

```python
from contextlib import ExitStack

import numpy as np

import concourse.bass as bass
from concourse import mybir

F32 = mybir.dt.float32
F32R = mybir.dt.float32r
U32 = mybir.dt.uint32
ALU = mybir.AluOpType
ACT = mybir.ActivationFunctionType

P = 128
BATCH = 2048
F = 32
D = 64
NB = 256
BLOCKS = BATCH // NB
BANK = 512
SUB = NB // P
PAIRS = F // 2
H1, H2 = 512, 256

TILES = [(i, k) for i in range(F - 2, -1, -1) for k in range((i + 1) // 2, PAIRS)]
UNIT = 4
UNITS = len(TILES) // UNIT
ROUNDS = 16
CHUNKS = UNITS // ROUNDS
LSLOTS, PSLOTS = 2, 4
SSLOTS = 6
RAWS = 4
EARLY = 5
WTILES = 4
WCHUNKS = len(TILES) // WTILES
WSTAGES = 5
MLPS = H1 // P + H2 // P + 1

FIRST = {i: min(q for q, t in enumerate(TILES) if t[0] == i) // UNIT for i in range(F - 1)}
LAST = {i: max(q for q, t in enumerate(TILES) if t[0] == i) // UNIT for i in range(F - 1)}

ZROW = {}
for c in range(CHUNKS):
    units = sorted(range(c * ROUNDS, (c + 1) * ROUNDS),
                   key=lambda r: all(2 * k != i for i, k in TILES[r * UNIT:(r + 1) * UNIT]))
    for s, r in enumerate(units):
        order = sorted(range(r * UNIT, (r + 1) * UNIT), key=lambda q: 2 * TILES[q][1] == TILES[q][0])
        for g, q in enumerate(order):
            ZROW[q] = c * P + 32 * g + 2 * s
ZERO_ROWS = sorted(ZROW[q] for q, (i, k) in enumerate(TILES) if 2 * k == i)
DENSE_RUNS = []
for m, row in enumerate(ZERO_ROWS):
    if m and row == ZERO_ROWS[m - 1] + 2 and row // P == ZERO_ROWS[m - 1] // P:
        DENSE_RUNS[-1][2] += 1
    else:
        DENSE_RUNS.append([row, m, 1])


def slot(i):
    return 0 if i == F - 2 else 1 + i % (SSLOTS - 1)


def had_slot(i):
    if i == F - 2:
        return i, False
    return (i + SSLOTS - 1, True) if i + SSLOTS - 1 < F - 2 else (i % (SSLOTS - 1), False)


FAST = 2 * (PAIRS - EARLY)
FASTS = F - 1 - FAST
SLOWS = PAIRS - EARLY

SPLIT_AT, TURN_AT, HIGH_AT, LOW_AT = {}, [-12, -9, -7, -5, -3], {}, {}
for i in range(F - 2, -1, -1):
    n = PAIRS - 1 - i // 2
    who, same = had_slot(i)
    had = LAST[who] if same else LAST[who] - UNITS
    SPLIT_AT[i] = max(FIRST[i] - 6, had, SPLIT_AT.get(i + 1, -UNITS))
    if i < FAST:
        if i % 2:
            TURN_AT.append(max(SPLIT_AT[i] - 5, 2 * n - 9))
            HIGH_AT[n] = max(SPLIT_AT[i] - 2, TURN_AT[n] + 1)
            LOW_AT[n] = HIGH_AT[n] + 1
        SPLIT_AT[i] = max(SPLIT_AT[i], LOW_AT[n] + 1)
FAST_LOW_AT = {i: SPLIT_AT[i] + 1 for i in range(F - 2, FAST - 1, -1)}
NEED = [n * n // UNIT for n in range(PAIRS)]
TURN_AT0 = [min(max(0, u - (1 if u < 16 else 2)), UNITS + TURN_AT[0] - 2) for u in NEED]
HIGH_AT0 = {n: TURN_AT0[n] for n in HIGH_AT}
SPLIT_AT0 = {i: TURN_AT0[PAIRS - 1 - i // 2] for i in SPLIT_AT}
FAST_LOW_AT0 = {i: SPLIT_AT0[i] for i in FAST_LOW_AT}

W_AT = [min(max(0, c * UNITS // WCHUNKS - 10), int(0.7 * c * UNITS / WCHUNKS)) for c in range(WCHUNKS)]


def prior_low(n):
    return (n - 2, True) if n - 2 >= EARLY else (PAIRS - 1 - (PAIRS - 1 - n) % 2, False)


L1_AT, L2_AT, L3_AT = 10, 16, 20


def at(places, places0, r, first, last):
    own = places0 if first else places
    fast_first = isinstance(places, dict) and max(places) > PAIRS
    order = sorted(places if isinstance(places, dict) else range(len(places)), reverse=fast_first)
    due = [(n, 0) for n in order if own[n] == r]
    if not last:
        due += [(n, 1) for n in order if places[n] < 0 and places[n] + UNITS == r]
    return due


def dlrm_kernel(nc, ids, tables, w_pairs, dense_t, w_top1, b_top1, w_top2, b_top2, w_top3,
                ident_in, sel_in, out):
    ctx = ExitStack()
    with ctx:
        def sb(name, cols, dt=F32):
            return ctx.enter_context(nc.sbuf_tensor(name, [P, cols], dt))

        def ps(name, cols):
            return ctx.enter_context(nc.psum_tensor(name, [P, cols], F32))

        def sem(name):
            return ctx.enter_context(nc.semaphore(name))

        w_split = sb("w_split", len(TILES) * P, F32R)
        late = sb("late", (EARLY + H1 // P + H2 // P) * NB)
        x_main = sb("x_main", PAIRS * NB)
        raw = sb("raw", RAWS * SUB * P)
        x_high = sb("x_high", NB, F32R)
        x_low = sb("x_low", 2 * NB)
        s_high = sb("s_high", SSLOTS * NB, F32R)
        s_low = sb("s_low", SSLOTS * NB, F32R)
        prods = sb("prods", PSLOTS * UNIT * NB)
        z = sb("z", CHUNKS * NB)
        w1 = sb("w1", CHUNKS * H1)
        w2 = sb("w2", (H1 // P) * H2)
        w3 = sb("w3", H2 // P)
        b1 = sb("b1", H1 // P)
        b2 = sb("b2", H2 // P)
        ident = sb("ident", P)
        sel = sb("sel", 62)
        idx = sb("idx", 2 * SUB * F, U32)
        h1 = late[:, EARLY * NB:(EARLY + H1 // P) * NB]
        h2 = late[:, (EARLY + H1 // P) * NB:]
        y = h2[0:1, 0:NB]
        wcols = WTILES * P

        left = ps("left", LSLOTS * UNIT * NB)
        z_sum = ps("z_sum", 2 * BANK)
        turned = ps("turned", BANK)
        mlp = ps("mlp", BANK)

        consts_in = sem("consts_in")
        top_in = sem("top_in")
        ids_in = sem("ids_in")
        slot_free = sem("slot_free")
        dense_in = sem("dense_in")
        gathered = [sem(f"gathered{s}") for s in range(RAWS)]
        w_in = [sem(f"w_in{s}") for s in range(WSTAGES)]
        w_rounded = sem("w_rounded")
        w_ready = sem("w_ready")
        x_turned = sem("x_turned")
        x_ready = sem("x_ready")
        high_ready = sem("high_ready")
        low_ready = sem("low_ready")
        s_ready = sem("s_ready")
        fast_ready = sem("fast_ready")
        left_ready = sem("left_ready")
        prods_ready = sem("prods_ready")
        prods_summed = sem("prods_summed")
        z_ready = sem("z_ready")
        mlp_out = sem("mlp_out")
        mlp_taken = sem("mlp_taken")
        y_out = sem("y_out")

        def x_at(k, parity):
            if parity and k >= PAIRS - EARLY:
                return late, (k - (PAIRS - EARLY)) * NB
            return x_main, k * NB

        def x_pair(k, parity):
            tensor, c = x_at(k, parity)
            return tensor[:, c:c + NB]

        def before(sem_count, first, count):
            return not first or sem_count + count > 0

        block = ctx.enter_context(nc.Block())

        @block.sync
        def _(sp):
            sp.dma_start(ident[:, :], ident_in).then_inc(consts_in, 16)
            sp.dma_start(sel[:, :], sel_in).then_inc(consts_in, 16)
            for c in range(WCHUNKS):
                stage = late[:, (c % WSTAGES) * wcols:(c % WSTAGES + 1) * wcols]
                if c >= WSTAGES:
                    sp.wait_ge(w_ready, c - WSTAGES + 1)
                twice = bass.AP(w_pairs.tensor, c * wcols, [[0, 2], [len(TILES) * P, D], [1, wcols]])
                sp.dma_start(stage, twice).then_inc(w_in[c % WSTAGES], 16)
            sp.dma_start(w1[:, :].rearrange("p (c n) -> p c n", c=CHUNKS),
                         w_top1.rearrange("(c p) n -> p c n", p=P)).then_inc(top_in, 16)
            sp.dma_start(w2[:, :].rearrange("p (c n) -> p c n", c=H1 // P),
                         w_top2.rearrange("(c p) n -> p c n", p=P)).then_inc(top_in, 16)
            sp.dma_start(w3[:, :], w_top3).then_inc(top_in, 16)
            sp.dma_start(b1[:, :], b_top1).then_inc(top_in, 16)
            sp.dma_start(b2[:, :], b_top2).then_inc(top_in, 16)
            with sp.Fori(0, BLOCKS) as t:
                for row, m, n in DENSE_RUNS:
                    p, c = row % P, row // P
                    sp.wait_ge(z_ready, t * CHUNKS + (c + 1))
                    sp.dma_start(z[p:p + 2 * n - 1:2, c * NB:(c + 1) * NB],
                                 dense_t[m:m + n, bass.ds(t * NB, NB)]).then_inc(dense_in, 16)
                sp.wait_ge(mlp_taken, t * MLPS + MLPS)
                sp.dma_start(out[:, bass.ds(t * NB, NB)], y).then_inc(y_out, 16)
            sp.wait_ge(y_out, 16 * BLOCKS)

        @block.gpsimd
        def _(pool):
            def load_indices(t, parity):
                src = ids[t] if isinstance(t, int) else ids[bass.ds(t, 1), :, :].rearrange("a p c -> (a p) c")
                pool.dma_start(idx[:, parity * SUB * F:(parity + 1) * SUB * F], src).then_inc(ids_in, 16)

            def gather_block(t, parity, first=False, last=False):
                pool.wait_ge(ids_in, t * 16 + 16)
                for n in range(PAIRS):
                    if not first or n >= RAWS:
                        pool.wait_ge(x_turned, t * PAIRS + (n - RAWS + 1))
                    pool.sem_inc(slot_free, 1)
                    for h in range(2):
                        f = 2 * (PAIRS - 1 - n) + h
                        for s in range(SUB):
                            c = ((n % RAWS) * SUB + s) * P + h * D
                            i = (parity * F + f) * SUB + s
                            pool.indirect_dma_start(
                                raw[:, c:c + D], None, tables[f],
                                bass.IndirectOffsetOnAxis(ap=idx[:, i:i + 1], axis=0),
                            ).then_inc(gathered[n % RAWS], 16)
                    if n == RAWS + 1 and not last:
                        load_indices(t + 1, 1 - parity)

            load_indices(0, 0)
            gather_block(0, 0, first=True)
            with pool.Fori(0, BLOCKS // 2 - 1) as two:
                gather_block(two * 2 + 1, 1)
                gather_block(two * 2 + 2, 0)
            gather_block(BLOCKS - 1, 1, last=True)

        @block.tensor
        def _(pe):
            def turn(t, n, ahead):
                g = (t + ahead) * PAIRS + n
                pe.wait_ge(gathered[n % RAWS], (t + ahead) * (PAIRS // RAWS * 2 * SUB * 16)
                           + (n // RAWS + 1) * 2 * SUB * 16)
                if not isinstance(g, int) or g >= 1:
                    pe.wait_ge(x_ready, g)
                for s in range(SUB):
                    c = ((n % RAWS) * SUB + s) * P
                    last = nc.tensor.transpose(turned[:, s * P:(s + 1) * P],
                                               raw[:, c:c + P], ident[:, :])
                last.then_inc(x_turned, 1)

            def multiply(t, r, first):
                if first and r % (WTILES // UNIT) == 0:
                    pe.wait_ge(w_ready, r // (WTILES // UNIT) + 1)
                if not first or r >= LSLOTS:
                    pe.wait_ge(prods_ready, t * UNITS + (r - LSLOTS + 1))
                for a in range(UNIT):
                    q = r * UNIT + a
                    i = TILES[q][0]
                    if a == 0 or i != TILES[q - 1][0]:
                        pe.wait_ge(s_ready, t * (F - 1) + (F - 1 - i))
                        if i >= FAST:
                            pe.wait_ge(fast_ready, t * FASTS + (F - 1 - i))
                    o = left[:, ((r % LSLOTS) * UNIT + a) * NB:((r % LSLOTS) * UNIT + a + 1) * NB]
                    w = w_split[:, q * P:(q + 1) * P]
                    c = slot(i) * NB
                    nc.tensor.matmul(o, w, s_high[:, c:c + NB], start=True, stop=False)
                    last = nc.tensor.matmul(o, w, s_low[:, c:c + NB], start=False, stop=True)
                last.then_inc(left_ready, 1)

            def reduce(t, r, first):
                c, s = divmod(r, ROUNDS)
                if s == 0 and (not first or c >= 2):
                    pe.wait_ge(z_ready, t * CHUNKS + (c - 1))
                pe.wait_ge(prods_ready, t * UNITS + (r + 1))
                for q in sorted(range(r * UNIT, (r + 1) * UNIT), key=ZROW.get):
                    g, row = divmod(ZROW[q] % P, 32)
                    a = (r % PSLOTS) * UNIT + q % UNIT
                    last = nc.tensor.matmul(z_sum[32 * g:32 * g + 32, (c % 2) * BANK:(c % 2) * BANK + NB],
                                            sel[:, 30 - row:62 - row], prods[:, a * NB:(a + 1) * NB],
                                            start=(s == 0), stop=(s == ROUNDS - 1))
                last.then_inc(prods_summed, 1)

            def layer1(t, j, once):
                if j == 0:
                    if once:
                        pe.wait_ge(top_in, 16 * 5)
                    pe.wait_ge(z_ready, t * CHUNKS + CHUNKS)
                    pe.wait_ge(dense_in, (t * 16 + 16) * len(DENSE_RUNS))
                if not once or j:
                    pe.wait_ge(mlp_taken, t * MLPS + j)
                for c in range(CHUNKS):
                    last = nc.tensor.matmul(mlp[:, 0:NB], w1[:, c * H1 + j * P:c * H1 + (j + 1) * P],
                                            z[:, c * NB:(c + 1) * NB], start=(c == 0), stop=(c == CHUNKS - 1))
                last.then_inc(mlp_out, 1)

            def layer2(t, j):
                pe.wait_ge(mlp_taken, t * MLPS + (H1 // P + j))
                for c in range(H1 // P):
                    last = nc.tensor.matmul(mlp[:, 0:NB], w2[:, c * H2 + j * P:c * H2 + (j + 1) * P],
                                            h1[:, c * NB:(c + 1) * NB], start=(c == 0), stop=(c == H1 // P - 1))
                last.then_inc(mlp_out, 1)

            def layer3(t):
                pe.wait_ge(mlp_taken, t * MLPS + H1 // P + H2 // P)
                for c in range(H2 // P):
                    last = nc.tensor.matmul(mlp[0:1, 0:NB], w3[:, c:c + 1], h2[:, c * NB:(c + 1) * NB],
                                            start=(c == 0), stop=(c == H2 // P - 1))
                last.then_inc(mlp_out, 1)

            def top(t, r, once):
                if L1_AT <= r < L1_AT + H1 // P:
                    layer1(t, r - L1_AT, once)
                if L2_AT <= r < L2_AT + H2 // P:
                    layer2(t, r - L2_AT)
                if r == L3_AT:
                    layer3(t)

            def run_block(t, first=False, last=False, once=False):
                for r in range(UNITS):
                    for n, ahead in at(TURN_AT, TURN_AT0, r, first, last):
                        turn(t, n, ahead)
                    multiply(t, r, first)
                    if r % 2:
                        for d in (3, 2):
                            if r >= d:
                                reduce(t, r - d, first)
                            elif not first:
                                reduce(t - 1, r - d + UNITS, once)
                    if not first:
                        top(t - 1, r, once)

            pe.wait_ge(consts_in, 32)
            run_block(0, first=True)
            run_block(1, once=True)
            with pe.Fori(2, BLOCKS - 1) as t:
                run_block(t)
            run_block(BLOCKS - 1, last=True)
            for r in (UNITS - 2, UNITS - 1):
                reduce(BLOCKS - 1, r, False)
            for r in range(UNITS):
                top(BLOCKS - 1, r, False)

        @block.scalar
        def _(act):
            def round_w(c):
                act.wait_ge(w_in[c % WSTAGES], (c // WSTAGES + 1) * 16)
                nc.scalar.copy(w_split[:, c * wcols:(c + 1) * wcols],
                               late[:, (c % WSTAGES) * wcols:(c % WSTAGES + 1) * wcols]).then_inc(w_rounded, 1)

            def take_x(t, n, ahead, parity, first):
                k = PAIRS - 1 - n
                g = (t + ahead) * PAIRS + n
                act.wait_ge(x_turned, g + 1)
                if ahead and first:
                    act.wait_ge(w_ready, WCHUNKS)
                elif not first:
                    act.wait_ge(prods_ready, (t - 1 + ahead) * UNITS if ahead else t * UNITS)
                nc.scalar.copy(x_pair(k, (parity + ahead) % 2), turned[:, 0:NB])\
                    .then_inc(x_ready, 1)

            def high(t, n, ahead, parity):
                g = (t + ahead) * SLOWS + (n - EARLY)
                act.wait_ge(x_ready, (t + ahead) * PAIRS + (n + 1))
                if not isinstance(g, int) or g >= 1:
                    act.wait_ge(low_ready, g)
                nc.scalar.copy(x_high[:, :], x_pair(PAIRS - 1 - n, (parity + ahead) % 2)).then_inc(high_ready, 1)

            def split(t, i, ahead, parity, first):
                n = PAIRS - 1 - i // 2
                x = x_pair(i // 2, (parity + ahead) % 2)
                c = slot(i) * NB
                rows = slice(D, P) if i % 2 else slice(0, D)
                who, same = had_slot(i)
                if same:
                    act.wait_ge(left_ready, (t + ahead) * UNITS + (LAST[who] + 1))
                elif not (first and not ahead):
                    act.wait_ge(left_ready, (t + ahead) * UNITS + (LAST[who] + 1 - UNITS))
                act.wait_ge(x_ready, (t + ahead) * PAIRS + (n + 1))
                nc.scalar.copy(s_high[0:D, c:c + NB], x[rows, :])
                last = nc.scalar.copy(s_high[D:P, c:c + NB], x[rows, :])
                if i < FAST:
                    act.wait_ge(low_ready, (t + ahead) * SLOWS + (n - EARLY + 1))
                    low = x_low[rows, (n % 2) * NB:(n % 2 + 1) * NB]
                    nc.scalar.copy(s_low[0:D, c:c + NB], low)
                    last = nc.scalar.copy(s_low[D:P, c:c + NB], low)
                last.then_inc(s_ready, 1)

            def take_z(t, c, once):
                act.wait_ge(prods_summed, t * UNITS + (c + 1) * ROUNDS)
                if not once:
                    act.wait_ge(mlp_out, (t - 1) * MLPS + H1 // P)
                nc.scalar.copy(z[:, c * NB:(c + 1) * NB], z_sum[:, (c % 2) * BANK:(c % 2) * BANK + NB])\
                    .then_inc(z_ready, 1)

            def relu(t, m, once):
                act.wait_ge(mlp_out, t * MLPS + (m + 1))
                if once and m == 0:
                    act.wait_ge(w_ready, WCHUNKS)
                if m < H1 // P:
                    nc.scalar.activation(h1[:, m * NB:(m + 1) * NB], mlp[:, 0:NB], ACT.Relu, bias=b1[:, m:m + 1])\
                        .then_inc(mlp_taken, 1)
                else:
                    j = m - H1 // P
                    if not once:
                        act.wait_ge(y_out, t * 16)
                    nc.scalar.activation(h2[:, j * NB:(j + 1) * NB], mlp[:, 0:NB], ACT.Relu, bias=b2[:, j:j + 1]).then_inc(mlp_taken, 1)

            def take_y(t, once):
                act.wait_ge(mlp_out, t * MLPS + MLPS)
                nc.scalar.copy(y, mlp[0:1, 0:NB]).then_inc(mlp_taken, 1)

            def top(t, r, once):
                if L1_AT + 1 <= r < L1_AT + 1 + H1 // P:
                    relu(t, r - L1_AT - 1, once)
                if L2_AT + 1 <= r < L2_AT + 1 + H2 // P:
                    relu(t, r - L2_AT - 1 + H1 // P, once)
                if r == L3_AT + 1:
                    take_y(t, once)

            def run_block(t, parity, first=False, last=False, once=False):
                for r in range(UNITS):
                    if first:
                        for c in range(WCHUNKS):
                            if W_AT[c] == r:
                                round_w(c)
                    for n, ahead in at(TURN_AT, TURN_AT0, r, first, last):
                        take_x(t, n, ahead, parity, first)
                    highs = at(HIGH_AT, HIGH_AT0, r, first, last)
                    splits = at(SPLIT_AT, SPLIT_AT0, r, first, last)
                    for i, ahead in splits:
                        if (PAIRS - 1 - i // 2, ahead) not in highs:
                            split(t, i, ahead, parity, first)
                    for n, ahead in highs:
                        high(t, n, ahead, parity)
                        for i, far in splits:
                            if (PAIRS - 1 - i // 2, far) == (n, ahead):
                                split(t, i, far, parity, first)
                    if r == 2 and not first:
                        take_z(t - 1, CHUNKS - 1, once)
                    if r > 2 and r % ROUNDS == 2:
                        take_z(t, r // ROUNDS - 1, first)
                    if not first:
                        top(t - 1, r, once)

            run_block(0, 0, first=True)
            run_block(1, 1, once=True)
            with act.Fori(2, BLOCKS - 2, 2) as t:
                run_block(t, 0)
                run_block(t + 1, 1)
            run_block(BLOCKS - 2, 0)
            run_block(BLOCKS - 1, 1, last=True)
            take_z(BLOCKS - 1, CHUNKS - 1, False)
            for r in range(UNITS):
                top(BLOCKS - 1, r, False)

        @block.vector
        def _(dve):
            def split_w(c):
                dve.wait_ge(w_rounded, c + 1)
                cols = slice(c * wcols, (c + 1) * wcols)
                nc.vector.tensor_tensor(w_split[D:P, cols],
                                        late[D:P, (c % WSTAGES) * wcols:(c % WSTAGES + 1) * wcols],
                                        w_split[D:P, cols].bitcast(F32), ALU.subtract).then_inc(w_ready, 1)

            def low(t, n, ahead, parity, first):
                dve.wait_ge(high_ready, (t + ahead) * SLOWS + (n - EARLY + 1))
                had, same = prior_low(n)
                if same or not (first and not ahead):
                    dve.wait_ge(s_ready, (t + ahead) * (F - 1) + (2 * had + 1 - (0 if same else F - 1)))
                nc.vector.tensor_tensor(x_low[:, (n % 2) * NB:(n % 2 + 1) * NB],
                                        x_pair(PAIRS - 1 - n, (parity + ahead) % 2),
                                        x_high[:, :].bitcast(F32), ALU.subtract).then_inc(low_ready, 1)

            def fast_low(t, i, ahead, parity):
                x = x_pair(i // 2, (parity + ahead) % 2)
                c = slot(i) * NB
                rows = slice(D, P) if i % 2 else slice(0, D)
                dve.wait_ge(s_ready, (t + ahead) * (F - 1) + (F - 1 - i))
                for half in (slice(0, D), slice(D, P)):
                    last = nc.vector.tensor_tensor(s_low[half, c:c + NB], x[rows, :],
                                                   s_high[rows, c:c + NB].bitcast(F32), ALU.subtract)
                last.then_inc(fast_ready, 1)

            def products(t, r, parity, first):
                dve.wait_ge(left_ready, t * UNITS + (r + 1))
                if not first or r >= PSLOTS:
                    dve.wait_ge(prods_summed, t * UNITS + (r - PSLOTS + 1))
                a = 0
                while a < UNIT:
                    tensor, c = x_at(TILES[r * UNIT + a][1], parity)
                    b = a + 1
                    while b < UNIT:
                        tb, cb = x_at(TILES[r * UNIT + b][1], parity)
                        if tb is not tensor or cb != c + (b - a) * NB:
                            break
                        b += 1
                    o, l = (r % PSLOTS) * UNIT, (r % LSLOTS) * UNIT
                    last = nc.vector.tensor_tensor(prods[:, (o + a) * NB:(o + b) * NB],
                                                   left[:, (l + a) * NB:(l + b) * NB],
                                                   tensor[:, c:c + (b - a) * NB], ALU.mult)
                    a = b
                last.then_inc(prods_ready, 1)

            def run_block(t, parity, first=False, last=False):
                for r in range(UNITS):
                    if first:
                        for c in range(WCHUNKS):
                            if W_AT[c] == r:
                                split_w(c)
                    for i, ahead in at(FAST_LOW_AT, FAST_LOW_AT0, r, first, last):
                        fast_low(t, i, ahead, parity)
                    for n, ahead in at(LOW_AT, HIGH_AT0, r, first, last):
                        low(t, n, ahead, parity, first)
                    products(t, r, parity, first)

            run_block(0, 0, first=True)
            with dve.Fori(1, BLOCKS - 1, 2) as t:
                run_block(t, 1)
                run_block(t + 1, 0)
            run_block(BLOCKS - 1, 1, last=True)


def pair_number(i, j):
    return i * (F - 1) - i * (i - 1) // 2 + (j - i - 1)


def kernel(**inputs):
    import concourse.bacc as bacc
    from concourse.bass_utils import run_bass_kernel_spmd

    w = inputs["L0_rec_W"]
    w_pairs = np.zeros((D, len(TILES), 2, D), w.dtype)
    w_top1 = np.zeros((CHUNKS * P, H1), w.dtype)
    for q, (i, k) in enumerate(TILES):
        for h in range(2):
            if 2 * k + h > i:
                p = pair_number(i, 2 * k + h)
                w_pairs[:, q, h, :] = w[p]
                w_top1[ZROW[q] + h] = inputs["W_top1"][p]
    w_top1[ZERO_ROWS] = inputs["W_top1"][F * (F - 1) // 2:]
    sel = np.zeros((P, 62), w.dtype)
    sel[:D, 30] = 1
    sel[D:, 31] = 1
    ids = np.ascontiguousarray(inputs["ids"].reshape(BLOCKS, SUB, P, F).transpose(0, 2, 3, 1))
    arrays = {
        "ids": ids.reshape(BLOCKS, P, F * SUB),
        "w_pairs": w_pairs.reshape(D, len(TILES) * P),
        "dense_t": np.ascontiguousarray(inputs["dense_ctx"].T),
        "w_top1": w_top1,
        "b_top1": np.ascontiguousarray(inputs["b_top1"].reshape(H1 // P, P).T),
        "w_top2": np.ascontiguousarray(inputs["W_top2"]),
        "b_top2": np.ascontiguousarray(inputs["b_top2"].reshape(H2 // P, P).T),
        "w_top3": np.ascontiguousarray(inputs["W_top3"].reshape(H2 // P, P).T),
        "ident": np.eye(P, dtype=w.dtype),
        "sel": sel,
    }
    for f in range(F):
        arrays[f"tbl_{f}"] = np.ascontiguousarray(inputs[f"tbl_{f}"])
    nc = bacc.Bacc("TRN2", target_bir_lowering=False, num_devices=1)
    ap = {}
    for name, a in arrays.items():
        dt = U32 if name == "ids" else mybir.dt.from_np(a.dtype)
        ap[name] = nc.dram_tensor(f"in_{name}", a.shape, dt, kind="ExternalInput").ap()
    out = nc.dram_tensor("out_y", (1, BATCH), F32, kind="ExternalOutput").ap()
    dlrm_kernel(nc, ap["ids"], [ap[f"tbl_{f}"] for f in range(F)], ap["w_pairs"], ap["dense_t"], ap["w_top1"],
                ap["b_top1"], ap["w_top2"], ap["b_top2"], ap["w_top3"], ap["ident"], ap["sel"], out)
    arrays["ids"] = arrays["ids"].view(np.uint32)
    result = run_bass_kernel_spmd(nc, [{f"in_{k}": v for k, v in arrays.items()}], core_ids=[0])
    return result.results[0]["out_y"].reshape(BATCH, 1)
```

```python
from contextlib import ExitStack

import numpy as np

import concourse.bass as bass
from concourse import mybir

F32 = mybir.dt.float32
F32R = mybir.dt.float32r
U32 = mybir.dt.uint32
ALU = mybir.AluOpType
ACT = mybir.ActivationFunctionType

P = 128
BATCH = 2048
F = 32
D = 64
NB = 256
BLOCKS = BATCH // NB
BANK = 512
SUB = NB // P
PAIRS = F // 2
H1, H2 = 512, 256

ORDER = [23, 29, 22, 28, 30, 27, 21, 20, 26, *range(19, 11, -1), 25, 24, *range(11, -1, -1)]
TILES = [(i, k) for i in ORDER for k in range((i + 1) // 2, PAIRS)]
UNIT = 4
UNITS = len(TILES) // UNIT
ROUNDS = 16
HALVES = UNITS // (2 * ROUNDS)
CHUNKS = 2 * HALVES
LSLOTS, PSLOTS = 2, 4
SSLOTS = 6
RAWS = 4
EARLY = 5
FETCH = [11, 14, 15, 13, 12] + list(range(10, -1, -1))
WTILES = 4
WCHUNKS = len(TILES) // WTILES
WSTAGES = 5
MLPS = H1 // P + H2 // P + 1

FIRST = {i: min(q for q, t in enumerate(TILES) if t[0] == i) // UNIT for i in range(F - 1)}
LAST = {i: max(q for q, t in enumerate(TILES) if t[0] == i) // UNIT for i in range(F - 1)}

def has_zero(r):
    return any(2 * k == i for i, k in TILES[r * UNIT:(r + 1) * UNIT])


ZROW = {}
for half in range(HALVES):
    twos = sorted(range(half * ROUNDS, (half + 1) * ROUNDS),
                  key=lambda m: {(1, 0): 0, (1, 1): 1, (0, 1): 2, (0, 0): 3}[has_zero(2 * m), has_zero(2 * m + 1)])
    for s, m in enumerate(twos):
        for r in (2 * m, 2 * m + 1):
            order = sorted(range(r * UNIT, (r + 1) * UNIT), key=lambda q: 2 * TILES[q][1] == TILES[q][0])
            for g, q in enumerate(order):
                ZROW[q] = (2 * half + r % 2) * P + 32 * g + 2 * s
ZERO_ROWS = sorted(ZROW[q] for q, (i, k) in enumerate(TILES) if 2 * k == i)
DENSE_RUNS = []
for m, row in enumerate(ZERO_ROWS):
    if m and row == ZERO_ROWS[m - 1] + 2 and row // P == ZERO_ROWS[m - 1] // P:
        DENSE_RUNS[-1][2] += 1
    else:
        DENSE_RUNS.append([row, m, 1])


def slot(i):
    return 0 if i == ORDER[0] else 1 + ORDER.index(i) % (SSLOTS - 1)


def had_slot(i):
    at = ORDER.index(i)
    if at == 0:
        return i, False
    return (ORDER[at - SSLOTS + 1], True) if at >= SSLOTS else (ORDER[at + F - 1 - SSLOTS], False)


JOBS = list(dict.fromkeys(i // 2 for i in ORDER))
TURN_AT = {FETCH[n]: 2 * n - 17 for n in range(EARLY)}
HIGH_AT, LOW_AT, SPLIT_AT = {}, {}, {}
for i in ORDER:
    k = i // 2
    who, same = had_slot(i)
    had = LAST[who] if same else LAST[who] - UNITS
    ready = max([FIRST[i] - 10, had, *SPLIT_AT.values()])
    if k not in HIGH_AT:
        if k not in TURN_AT:
            TURN_AT[k] = max([0, ready - 4, *(p + 2 for p in TURN_AT.values())])
        HIGH_AT[k] = max([TURN_AT[k] + 1, ready - 2, *HIGH_AT.values()])
        LOW_AT[k] = HIGH_AT[k] + 1
    SPLIT_AT[i] = max(ready, LOW_AT[k])

NEED = {k: min(FIRST[i] for i in ORDER if i // 2 == k) for k in JOBS}
TURN_AT0 = {k: 0 if n < EARLY else min(NEED[k] - 2, 49, 2 + 27 * (n - EARLY) // 10) for n, k in enumerate(FETCH)}
HIGH_AT0, SPLIT_AT0 = {}, {}
for i in ORDER:
    who, same = had_slot(i)
    SPLIT_AT0[i] = max([TURN_AT0[i // 2], min(max(0, FIRST[i] - 3), 51), LAST[who] if same else 0,
                        *SPLIT_AT0.values()])
    HIGH_AT0.setdefault(i // 2, SPLIT_AT0[i])
LATER = 2

POOL_CHUNK = 48
PRELUDE = 22
W_AHEAD = [6, 11, 15, 18, 21]
W_AT = ([0] * PRELUDE + [1 + 5 * (c - PRELUDE) // 4 for c in range(PRELUDE, POOL_CHUNK)]
        + [min(c - 8, 34 + (c - POOL_CHUNK)) for c in range(POOL_CHUNK, WCHUNKS)])


MLP_AT = [14 + 4 * m for m in range(MLPS)]
TAKE_AT = {UNITS // 2 + 15: 0}


def at(places, places0, r, first, last):
    due = [(n, 0) for n in places if (places0 if first else places)[n] == r]
    if not last:
        due += [(n, 1) for n in places
                if places[n] < 0 and min(places[n] + UNITS + LATER * first, UNITS - 1) == r]
    return due


def dlrm_kernel(nc, ids, tables, w_pairs, dense_t, w_top1, b_top1, w_top2, b_top2, w_top3,
                ident_in, sel_in, out):
    ctx = ExitStack()
    with ctx:
        def sb(name, cols, dt=F32):
            return ctx.enter_context(nc.sbuf_tensor(name, [P, cols], dt))

        def ps(name, cols):
            return ctx.enter_context(nc.psum_tensor(name, [P, cols], F32))

        def sem(name):
            return ctx.enter_context(nc.semaphore(name))

        w_split = sb("w_split", len(TILES) * P, F32R)
        late = sb("late", (EARLY + H1 // P + H2 // P) * NB)
        x_main = sb("x_main", PAIRS * NB)
        raw = sb("raw", RAWS * SUB * P)
        x_high = sb("x_high", NB, F32R)
        x_low = sb("x_low", 2 * NB)
        s_high = sb("s_high", SSLOTS * NB, F32R)
        s_low = sb("s_low", SSLOTS * NB, F32R)
        prods = sb("prods", PSLOTS * UNIT * NB)
        z = sb("z", CHUNKS * NB)
        w1 = sb("w1", CHUNKS * H1)
        w2 = sb("w2", (H1 // P) * H2)
        w3 = sb("w3", H2 // P)
        b1 = sb("b1", H1 // P)
        b2 = sb("b2", H2 // P)
        ident = sb("ident", P)
        sel = sb("sel", 62)
        idx = sb("idx", 2 * SUB * F, U32)
        h1 = late[:, EARLY * NB:(EARLY + H1 // P) * NB]
        h2 = late[:, (EARLY + H1 // P) * NB:]
        y = h2[0:1, 0:NB]
        wcols = WTILES * P

        left = ps("left", LSLOTS * UNIT * NB)
        z_sum = ps("z_sum", 2 * BANK)
        turned = ps("turned", BANK)
        mlp = ps("mlp", BANK)

        def tail_bank(j):
            return (mlp, turned, left, left[:, BANK:])[j][:, 0:NB]

        consts_in = sem("consts_in")
        top_in = sem("top_in")
        ids_in = sem("ids_in")
        slot_free = sem("slot_free")
        dense_in = sem("dense_in")
        gathered = [sem(f"gathered{s}") for s in range(RAWS)]
        w_in = [sem(f"w_in{s}") for s in range(WSTAGES)]
        w_rounded = sem("w_rounded")
        w_ready = sem("w_ready")
        w_pooled = sem("w_pooled")
        x_turned = sem("x_turned")
        x_ready = sem("x_ready")
        high_ready = sem("high_ready")
        low_ready = sem("low_ready")
        s_ready = sem("s_ready")
        left_ready = sem("left_ready")
        prods_ready = sem("prods_ready")
        prods_summed = sem("prods_summed")
        z_ready = sem("z_ready")
        mlp_out = sem("mlp_out")
        mlp_taken = sem("mlp_taken")
        y_out = sem("y_out")

        def x_at(k, parity):
            if parity and k >= PAIRS - EARLY:
                return late, (k - (PAIRS - EARLY)) * NB
            return x_main, k * NB

        def x_pair(k, parity):
            tensor, c = x_at(k, parity)
            return tensor[:, c:c + NB]

        def wait_chunk(engine, c):
            if c < POOL_CHUNK:
                engine.wait_ge(w_ready, c + 1)
            else:
                engine.wait_ge(w_pooled, c - POOL_CHUNK + 1)

        def subtract_high(engine, c):
            engine.wait_ge(w_rounded, c + 1)
            cols = slice(c * wcols, (c + 1) * wcols)
            return engine.tensor_tensor(w_split[D:P, cols],
                                        late[D:P, (c % WSTAGES) * wcols:(c % WSTAGES + 1) * wcols],
                                        w_split[D:P, cols].bitcast(F32), ALU.subtract)

        block = ctx.enter_context(nc.Block())

        @block.sync
        def _(sp):
            sp.dma_start(ident[:, :], ident_in).then_inc(consts_in, 16)
            sp.dma_start(sel[:, :], sel_in).then_inc(consts_in, 16)
            for c in range(WCHUNKS):
                stage = late[:, (c % WSTAGES) * wcols:(c % WSTAGES + 1) * wcols]
                if c >= WSTAGES:
                    wait_chunk(sp, c - WSTAGES)
                twice = bass.AP(w_pairs.tensor, c * wcols, [[0, 2], [len(TILES) * P, D], [1, wcols]])
                sp.dma_start(stage, twice).then_inc(w_in[c % WSTAGES], 16)
            sp.dma_start(w1[:, :].rearrange("p (c n) -> p c n", c=CHUNKS),
                         w_top1.rearrange("(c p) n -> p c n", p=P)).then_inc(top_in, 16)
            sp.dma_start(w2[:, :].rearrange("p (c n) -> p c n", c=H1 // P),
                         w_top2.rearrange("(c p) n -> p c n", p=P)).then_inc(top_in, 16)
            sp.dma_start(w3[:, :], w_top3).then_inc(top_in, 16)
            sp.dma_start(b1[:, :], b_top1).then_inc(top_in, 16)
            sp.dma_start(b2[:, :], b_top2).then_inc(top_in, 16)
            with sp.Fori(0, BLOCKS) as t:
                for row, m, n in DENSE_RUNS:
                    p, c = row % P, row // P
                    sp.wait_ge(z_ready, t * HALVES + (c // 2 + 1))
                    sp.dma_start(z[p:p + 2 * n - 1:2, c * NB:(c + 1) * NB],
                                 dense_t[m:m + n, bass.ds(t * NB, NB)]).then_inc(dense_in, 16)
                sp.wait_ge(mlp_taken, t * MLPS + MLPS)
                sp.dma_start(out[:, bass.ds(t * NB, NB)], y).then_inc(y_out, 16)
            sp.wait_ge(y_out, 16 * BLOCKS)

        @block.gpsimd
        def _(pool):
            def load_indices(t, parity):
                src = ids[t] if isinstance(t, int) else ids[bass.ds(t, 1), :, :].rearrange("a p c -> (a p) c")
                pool.dma_start(idx[:, parity * SUB * F:(parity + 1) * SUB * F], src).then_inc(ids_in, 16)

            def gather_block(t, parity, first=False, last=False, pairs=range(PAIRS)):
                if 0 in pairs:
                    pool.wait_ge(ids_in, t * 16 + 16)
                for n in pairs:
                    if not first or n >= RAWS:
                        pool.wait_ge(x_turned, t * PAIRS + (n - RAWS + 1))
                    pool.sem_inc(slot_free, 1)
                    for h in range(2):
                        f = 2 * FETCH[n] + h
                        for s in range(SUB):
                            c = ((n % RAWS) * SUB + s) * P + h * D
                            i = (parity * F + f) * SUB + s
                            pool.indirect_dma_start(
                                raw[:, c:c + D], None, tables[f],
                                bass.IndirectOffsetOnAxis(ap=idx[:, i:i + 1], axis=0),
                            ).then_inc(gathered[n % RAWS], 16)
                    if n == RAWS + 1 and not last:
                        load_indices(t + 1, 1 - parity)

            load_indices(0, 0)
            gather_block(0, 0, first=True)
            gather_block(1, 1, pairs=range(RAWS))
            for s in range(RAWS):
                pool.wait_ge(gathered[s], (PAIRS // RAWS + 1) * 2 * SUB * 16)
            for c in range(POOL_CHUNK, WCHUNKS):
                subtract_high(nc.gpsimd, c).then_inc(w_pooled, 1)
            pool.wait_ge(w_pooled, WCHUNKS - POOL_CHUNK)
            gather_block(1, 1, pairs=range(RAWS, PAIRS))
            with pool.Fori(1, BLOCKS // 2 - 1) as two:
                gather_block(two * 2, 0)
                gather_block(two * 2 + 1, 1)
            gather_block(BLOCKS - 2, 0)
            gather_block(BLOCKS - 1, 1, last=True)

        @block.tensor
        def _(pe):
            def turn(t, k, ahead):
                n = FETCH.index(k)
                g = (t + ahead) * PAIRS + n
                pe.wait_ge(gathered[n % RAWS], (t + ahead) * (PAIRS // RAWS * 2 * SUB * 16)
                           + (n // RAWS + 1) * 2 * SUB * 16)
                if not isinstance(g, int) or g >= 1:
                    pe.wait_ge(x_ready, g)
                for s in range(SUB):
                    c = ((n % RAWS) * SUB + s) * P
                    last = nc.tensor.transpose(turned[:, s * P:(s + 1) * P],
                                               raw[:, c:c + P], ident[:, :])
                last.then_inc(x_turned, 1)

            def multiply(t, r, first):
                if first:
                    wait_chunk(pe, r)
                if not first or r >= LSLOTS:
                    pe.wait_ge(prods_ready, t * UNITS + (r - LSLOTS + 1))
                for a in range(UNIT):
                    q = r * UNIT + a
                    i = TILES[q][0]
                    if a == 0 or i != TILES[q - 1][0]:
                        pe.wait_ge(s_ready, t * (F - 1) + (ORDER.index(i) + 1))
                    o = left[:, ((r % LSLOTS) * UNIT + a) * NB:((r % LSLOTS) * UNIT + a + 1) * NB]
                    w = w_split[:, q * P:(q + 1) * P]
                    c = slot(i) * NB
                    nc.tensor.matmul(o, w, s_high[:, c:c + NB], start=True, stop=False)
                    last = nc.tensor.matmul(o, w, s_low[:, c:c + NB], start=False, stop=True)
                last.then_inc(left_ready, 1)

            def reduce(t, m, first):
                half, s = divmod(m, ROUNDS)
                if s == 0 and not first:
                    pe.wait_ge(z_ready, (t - 1) * HALVES + (half + 1))
                pe.wait_ge(prods_ready, t * UNITS + 2 * m + 2)
                even, odd = (sorted(range(r * UNIT, (r + 1) * UNIT), key=ZROW.get) for r in (2 * m, 2 * m + 1))
                slots = prods[:, :].rearrange("p (s n) -> p s n", n=NB)
                for g in range(UNIT):
                    row = ZROW[even[g]] % P - 32 * g
                    a = (2 * m % PSLOTS) * UNIT + even[g] % UNIT
                    b = ((2 * m + 1) % PSLOTS) * UNIT + odd[g] % UNIT
                    last = nc.tensor.matmul(z_sum[32 * g:32 * g + 32, half * BANK:half * BANK + 2 * NB],
                                            sel[:, 30 - row:62 - row], slots[:, a:b + 1:b - a, :],
                                            start=(s == 0), stop=(s == ROUNDS - 1))
                last.then_inc(prods_summed, 1)

            def layer1(t, j, once):
                if j == 0:
                    if once:
                        pe.wait_ge(top_in, 16 * 5)
                    pe.wait_ge(z_ready, t * HALVES + HALVES)
                    pe.wait_ge(dense_in, (t * 16 + 16) * len(DENSE_RUNS))
                if not once or j:
                    pe.wait_ge(mlp_taken, t * MLPS + j)
                for c in range(CHUNKS):
                    last = nc.tensor.matmul(mlp[:, 0:NB], w1[:, c * H1 + j * P:c * H1 + (j + 1) * P],
                                            z[:, c * NB:(c + 1) * NB], start=(c == 0), stop=(c == CHUNKS - 1))
                last.then_inc(mlp_out, 1)

            def layer2(t, j):
                pe.wait_ge(mlp_taken, t * MLPS + (H1 // P + j))
                for c in range(H1 // P):
                    last = nc.tensor.matmul(mlp[:, 0:NB], w2[:, c * H2 + j * P:c * H2 + (j + 1) * P],
                                            h1[:, c * NB:(c + 1) * NB], start=(c == 0), stop=(c == H1 // P - 1))
                last.then_inc(mlp_out, 1)

            def layer3(t):
                pe.wait_ge(mlp_taken, t * MLPS + H1 // P + H2 // P)
                for c in range(H2 // P):
                    last = nc.tensor.matmul(mlp[0:1, 0:NB], w3[:, c:c + 1], h2[:, c * NB:(c + 1) * NB],
                                            start=(c == 0), stop=(c == H2 // P - 1))
                last.then_inc(mlp_out, 1)

            def top(t, r, once):
                if r not in MLP_AT:
                    return
                m = MLP_AT.index(r)
                if m < H1 // P:
                    layer1(t, m, once)
                elif m < MLPS - 1:
                    layer2(t, m - H1 // P)
                else:
                    layer3(t)

            def run_block(t, first=False, last=False, once=False):
                for r in range(UNITS):
                    for k, ahead in at(TURN_AT, TURN_AT0, r, first, last):
                        turn(t, k, ahead)
                    multiply(t, r, first)
                    if r % 2 and r > 1:
                        reduce(t, r // 2 - 1, first)
                    elif r == 1 and not first:
                        reduce(t - 1, UNITS // 2 - 1, once)
                    if not first:
                        top(t - 1, r, once)

            def finish(t):
                def layer1_half(j, half):
                    for c in (2 * half, 2 * half + 1):
                        last = nc.tensor.matmul(tail_bank(j), w1[:, c * H1 + j * P:c * H1 + (j + 1) * P],
                                                z[:, c * NB:(c + 1) * NB], start=(c == 0), stop=(c == CHUNKS - 1))
                    return last

                pe.wait_ge(z_ready, t * HALVES + 1)
                pe.wait_ge(dense_in, t * 16 * len(DENSE_RUNS) + 16 * sum(row < 2 * P for row, _, _ in DENSE_RUNS))
                layer1_half(0, 0)
                layer1_half(1, 0)
                reduce(t, UNITS // 2 - 1, False)
                layer1_half(2, 0)
                layer1_half(3, 0)
                pe.wait_ge(z_ready, t * HALVES + HALVES)
                pe.wait_ge(dense_in, (t * 16 + 16) * len(DENSE_RUNS))
                for j in range(H1 // P):
                    layer1_half(j, 1).then_inc(mlp_out, 1)
                for j in range(H2 // P):
                    for c in range(H1 // P):
                        pe.wait_ge(mlp_taken, t * MLPS + max(c, j) + 1)
                        last = nc.tensor.matmul(tail_bank(j), w2[:, c * H2 + j * P:c * H2 + (j + 1) * P],
                                                h1[:, c * NB:(c + 1) * NB], start=(c == 0), stop=(c == H1 // P - 1))
                    last.then_inc(mlp_out, 1)
                for c in range(H2 // P):
                    pe.wait_ge(mlp_taken, t * MLPS + H1 // P + c + 1)
                    last = nc.tensor.matmul(tail_bank(2)[0:1, :], w3[:, c:c + 1], h2[:, c * NB:(c + 1) * NB],
                                            start=(c == 0), stop=(c == H2 // P - 1))
                last.then_inc(mlp_out, 1)

            pe.wait_ge(consts_in, 32)
            run_block(0, first=True)
            run_block(1, once=True)
            with pe.Fori(2, BLOCKS - 1) as t:
                run_block(t)
            run_block(BLOCKS - 1, last=True)
            finish(BLOCKS - 1)

        @block.scalar
        def _(act):
            def round_w(c):
                act.wait_ge(w_in[c % WSTAGES], (c // WSTAGES + 1) * 16)
                nc.scalar.copy(w_split[:, c * wcols:(c + 1) * wcols],
                               late[:, (c % WSTAGES) * wcols:(c % WSTAGES + 1) * wcols]).then_inc(w_rounded, 1)

            def take_x(t, k, ahead, parity, first):
                g = (t + ahead) * PAIRS + FETCH.index(k)
                act.wait_ge(x_turned, g + 1)
                if ahead and first:
                    wait_chunk(act, POOL_CHUNK - 1)
                    wait_chunk(act, WCHUNKS - 1)
                elif not first:
                    act.wait_ge(prods_ready, (t - 1 + ahead) * UNITS if ahead else t * UNITS)
                nc.scalar.copy(x_pair(k, (parity + ahead) % 2), turned[:, 0:NB])\
                    .then_inc(x_ready, 1)

            def high(t, k, ahead, parity):
                g = (t + ahead) * PAIRS + JOBS.index(k)
                act.wait_ge(x_ready, (t + ahead) * PAIRS + (FETCH.index(k) + 1))
                if not isinstance(g, int) or g >= 1:
                    act.wait_ge(low_ready, g)
                nc.scalar.copy(x_high[:, :], x_pair(k, (parity + ahead) % 2)).then_inc(high_ready, 1)

            def split(t, i, ahead, parity, first):
                x = x_pair(i // 2, (parity + ahead) % 2)
                job = JOBS.index(i // 2)
                c = slot(i) * NB
                rows = slice(D, P) if i % 2 else slice(0, D)
                who, same = had_slot(i)
                if same:
                    act.wait_ge(left_ready, (t + ahead) * UNITS + (LAST[who] + 1))
                elif not (first and not ahead):
                    act.wait_ge(left_ready, (t + ahead) * UNITS + (LAST[who] + 1 - UNITS))
                nc.scalar.copy(s_high[0:D, c:c + NB], x[rows, :])
                nc.scalar.copy(s_high[D:P, c:c + NB], x[rows, :])
                act.wait_ge(low_ready, (t + ahead) * PAIRS + (job + 1))
                low = x_low[rows, (job % 2) * NB:(job % 2 + 1) * NB]
                nc.scalar.copy(s_low[0:D, c:c + NB], low)
                nc.scalar.copy(s_low[D:P, c:c + NB], low).then_inc(s_ready, 1)

            def take_z(t, half, once):
                act.wait_ge(prods_summed, t * (UNITS // 2) + (half + 1) * ROUNDS)
                if not once:
                    act.wait_ge(mlp_out, (t - 1) * MLPS + H1 // P)
                nc.scalar.copy(z[:, half * 2 * NB:(half + 1) * 2 * NB], z_sum[:, half * BANK:half * BANK + 2 * NB])\
                    .then_inc(z_ready, 1)

            def relu(t, m, once, bank=None):
                bank = mlp[:, 0:NB] if bank is None else bank
                act.wait_ge(mlp_out, t * MLPS + (m + 1))
                if once and m == 0:
                    wait_chunk(act, WCHUNKS - 1)
                if m < H1 // P:
                    nc.scalar.activation(h1[:, m * NB:(m + 1) * NB], bank, ACT.Relu, bias=b1[:, m:m + 1])\
                        .then_inc(mlp_taken, 1)
                else:
                    j = m - H1 // P
                    if not once:
                        act.wait_ge(y_out, t * 16)
                    nc.scalar.activation(h2[:, j * NB:(j + 1) * NB], bank, ACT.Relu, bias=b2[:, j:j + 1])\
                        .then_inc(mlp_taken, 1)

            def take_y(t, bank=None):
                bank = mlp[:, 0:NB] if bank is None else bank
                act.wait_ge(mlp_out, t * MLPS + MLPS)
                nc.scalar.copy(y, bank[0:1, :]).then_inc(mlp_taken, 1)

            def top(t, r, once):
                if r - 1 not in MLP_AT:
                    return
                m = MLP_AT.index(r - 1)
                if m < MLPS - 1:
                    relu(t, m, once)
                else:
                    take_y(t)

            def prelude():
                for n in range(EARLY):
                    for c in range(W_AHEAD[n - 1] if n else 0, W_AHEAD[n]):
                        round_w(c)
                    k = FETCH[n]
                    take_x(0, k, 0, 0, True)
                    if HIGH_AT0[k] == 0:
                        high(0, k, 0, 0)
                        for i in ORDER:
                            if i // 2 == k and SPLIT_AT0[i] == 0:
                                split(0, i, 0, 0, True)
                for c in range(W_AHEAD[-1], PRELUDE):
                    round_w(c)

            def run_block(t, parity, first=False, last=False, once=False):
                if first:
                    prelude()
                for r in range(UNITS):
                    if first:
                        for c in range(PRELUDE, WCHUNKS):
                            if W_AT[c] == r:
                                round_w(c)
                    if first and r == 0:
                        continue
                    for k, ahead in at(TURN_AT, TURN_AT0, r, first, last):
                        take_x(t, k, ahead, parity, first)
                    highs = at(HIGH_AT, HIGH_AT0, r, first, last)
                    for i, ahead in at(SPLIT_AT, SPLIT_AT0, r, first, last):
                        while (i // 2, ahead) in highs:
                            high(t, *highs.pop(0), parity)
                        split(t, i, ahead, parity, first)
                    for k, ahead in highs:
                        high(t, k, ahead, parity)
                    if r == 2 and not first:
                        take_z(t - 1, HALVES - 1, once)
                    if r in TAKE_AT:
                        take_z(t, TAKE_AT[r], first)
                    if not first:
                        top(t - 1, r, once)

            run_block(0, 0, first=True)
            run_block(1, 1, once=True)
            with act.Fori(2, BLOCKS - 2, 2) as t:
                run_block(t, 0)
                run_block(t + 1, 1)
            run_block(BLOCKS - 2, 0)
            run_block(BLOCKS - 1, 1, last=True)
            take_z(BLOCKS - 1, HALVES - 1, False)
            for m in range(H1 // P):
                relu(BLOCKS - 1, m, False, tail_bank(m))
            for j in range(H2 // P):
                relu(BLOCKS - 1, H1 // P + j, False, tail_bank(j))
            take_y(BLOCKS - 1, tail_bank(2))

        @block.vector
        def _(dve):
            def low(t, k, ahead, parity, first):
                job = JOBS.index(k)
                dve.wait_ge(high_ready, (t + ahead) * PAIRS + (job + 1))
                done = 1 + max(ORDER.index(i) for i in ORDER if i // 2 == JOBS[job - 2])
                if job >= 2:
                    dve.wait_ge(s_ready, (t + ahead) * (F - 1) + done)
                elif not (first and not ahead):
                    dve.wait_ge(s_ready, (t + ahead) * (F - 1) + (done - (F - 1)))
                nc.vector.tensor_tensor(x_low[:, (job % 2) * NB:(job % 2 + 1) * NB],
                                        x_pair(k, (parity + ahead) % 2),
                                        x_high[:, :].bitcast(F32), ALU.subtract).then_inc(low_ready, 1)

            def products(t, r, parity, first):
                dve.wait_ge(left_ready, t * UNITS + (r + 1))
                if not first or r >= PSLOTS:
                    dve.wait_ge(prods_summed, t * (UNITS // 2) + ((r - PSLOTS) // 2 + 1))
                a = 0
                while a < UNIT:
                    tensor, c = x_at(TILES[r * UNIT + a][1], parity)
                    b = a + 1
                    while b < UNIT:
                        tb, cb = x_at(TILES[r * UNIT + b][1], parity)
                        if tb is not tensor or cb != c + (b - a) * NB:
                            break
                        b += 1
                    o, l = (r % PSLOTS) * UNIT, (r % LSLOTS) * UNIT
                    last = nc.vector.tensor_tensor(prods[:, (o + a) * NB:(o + b) * NB],
                                                   left[:, (l + a) * NB:(l + b) * NB],
                                                   tensor[:, c:c + (b - a) * NB], ALU.mult)
                    a = b
                last.then_inc(prods_ready, 1)

            def prelude():
                for n in range(EARLY):
                    for c in range(W_AHEAD[n - 1] if n else 0, W_AHEAD[n]):
                        subtract_high(nc.vector, c).then_inc(w_ready, 1)
                    if HIGH_AT0[FETCH[n]] == 0:
                        low(0, FETCH[n], 0, 0, True)
                for c in range(W_AHEAD[-1], PRELUDE):
                    subtract_high(nc.vector, c).then_inc(w_ready, 1)

            def run_block(t, parity, first=False, last=False):
                if first:
                    prelude()
                for r in range(UNITS):
                    if first:
                        for c in range(PRELUDE, POOL_CHUNK):
                            if W_AT[c] == r:
                                subtract_high(nc.vector, c).then_inc(w_ready, 1)
                    if not first or r:
                        for k, ahead in at(LOW_AT, HIGH_AT0, r, first, last):
                            low(t, k, ahead, parity, first)
                    products(t, r, parity, first)

            run_block(0, 0, first=True)
            with dve.Fori(1, BLOCKS - 1, 2) as t:
                run_block(t, 1)
                run_block(t + 1, 0)
            run_block(BLOCKS - 1, 1, last=True)


def pair_number(i, j):
    return i * (F - 1) - i * (i - 1) // 2 + (j - i - 1)


def kernel(**inputs):
    import concourse.bacc as bacc
    from concourse.bass_utils import run_bass_kernel_spmd

    w = inputs["L0_rec_W"]
    w_pairs = np.zeros((D, len(TILES), 2, D), w.dtype)
    w_top1 = np.zeros((CHUNKS * P, H1), w.dtype)
    for q, (i, k) in enumerate(TILES):
        for h in range(2):
            if 2 * k + h > i:
                p = pair_number(i, 2 * k + h)
                w_pairs[:, q, h, :] = w[p]
                w_top1[ZROW[q] + h] = inputs["W_top1"][p]
    w_top1[ZERO_ROWS] = inputs["W_top1"][F * (F - 1) // 2:]
    sel = np.zeros((P, 62), w.dtype)
    sel[:D, 30] = 1
    sel[D:, 31] = 1
    ids = np.ascontiguousarray(inputs["ids"].reshape(BLOCKS, SUB, P, F).transpose(0, 2, 3, 1))
    arrays = {
        "ids": ids.reshape(BLOCKS, P, F * SUB),
        "w_pairs": w_pairs.reshape(D, len(TILES) * P),
        "dense_t": np.ascontiguousarray(inputs["dense_ctx"].T),
        "w_top1": w_top1,
        "b_top1": np.ascontiguousarray(inputs["b_top1"].reshape(H1 // P, P).T),
        "w_top2": np.ascontiguousarray(inputs["W_top2"]),
        "b_top2": np.ascontiguousarray(inputs["b_top2"].reshape(H2 // P, P).T),
        "w_top3": np.ascontiguousarray(inputs["W_top3"].reshape(H2 // P, P).T),
        "ident": np.eye(P, dtype=w.dtype),
        "sel": sel,
    }
    for f in range(F):
        arrays[f"tbl_{f}"] = np.ascontiguousarray(inputs[f"tbl_{f}"])
    nc = bacc.Bacc("TRN2", target_bir_lowering=False, num_devices=1)
    ap = {}
    for name, a in arrays.items():
        dt = U32 if name == "ids" else mybir.dt.from_np(a.dtype)
        ap[name] = nc.dram_tensor(f"in_{name}", a.shape, dt, kind="ExternalInput").ap()
    out = nc.dram_tensor("out_y", (1, BATCH), F32, kind="ExternalOutput").ap()
    dlrm_kernel(nc, ap["ids"], [ap[f"tbl_{f}"] for f in range(F)], ap["w_pairs"], ap["dense_t"], ap["w_top1"],
                ap["b_top1"], ap["w_top2"], ap["b_top2"], ap["w_top3"], ap["ident"], ap["sel"], out)
    arrays["ids"] = arrays["ids"].view(np.uint32)
    result = run_bass_kernel_spmd(nc, [{f"in_{k}": v for k, v in arrays.items()}], core_ids=[0])
    return result.results[0]["out_y"].reshape(BATCH, 1)
```
